# Optimizing a Trainium2 kernel written in Bass

```python
import numpy as np
import jax
import jax.numpy as jnp

def _softmax(x, axis=-1):
    return jax.nn.softmax(x, axis=axis)

def _gelu(x):
    return jax.nn.gelu(x, approximate=True)

def _silu(x):
    return jax.nn.silu(x)

def _sigmoid(x):
    return jax.nn.sigmoid(x)

def _layernorm(x, axis=-1, eps=1e-05):
    m = jnp.mean(x, axis=axis, keepdims=True)
    v = jnp.var(x, axis=axis, keepdims=True)
    return (x - m) / jnp.sqrt(v + eps)

def _scatter_add(tgt, idx, src, axis=0):
    return tgt.at[idx].add(src)

def _segment_sum(src, seg, n):
    return jax.ops.segment_sum(src, seg, n)
kernel_name = 'mk_gnn_preln_d1_gnn_r8_6ca9d3'

def setup_inputs(seed: int=0):
    np.random.seed(seed)
    _w = jnp.asarray

    def _rec_inputs():
        import jax
        import jax.numpy as jnp
        _gk = jax.random.key(seed)
        x = -0.000202 + 1 * jax.random.normal(jax.random.fold_in(_gk, 1), (12500, 64), jnp.float32)
        src = jax.random.randint(jax.random.fold_in(_gk, 2), (200000,), 0, 12500, jnp.int32)
        dst = jnp.minimum((12500 * jax.random.uniform(jax.random.fold_in(_gk, 3), (200000,)) ** 2.0).astype(jnp.int32), 99999)
        _o = jnp.argsort(dst, stable=True)
        src = src[_o]
        dst = dst[_o]
        edge_attr_32 = 0.000196303 + 1.00016 * jax.random.normal(jax.random.fold_in(_gk, 11), (200000, 32), jnp.float32)
        return (x, src, dst, edge_attr_32)
    x, src, dst, edge_attr_32 = _rec_inputs()

    def _L0_gnn_setup():
        import jax, jax.numpy as jnp
        import numpy as np
        N, D, E, ED, L = (12500, 64, 100000, 32, 5)
        LN_EPS = 1e-05

        def _leaky(x):
            return jax.nn.leaky_relu(x, negative_slope=0.1)
        key = jax.random.key(seed)
        ks = jax.random.split(key, 16)
        s = 0.05
        return {'x': jax.random.normal(ks[0], (N, D), dtype=jnp.float32), 'edge_index': jax.random.randint(ks[1], (2, E), 0, N, dtype=jnp.int64), 'edge_attr': jax.random.normal(ks[2], (E, ED), dtype=jnp.float32), 'W1': jax.random.normal(ks[3], (L, D, 2 * D), dtype=jnp.float32) * s, 'b1': jnp.zeros((L, 2 * D), dtype=jnp.float32), 'W2': jax.random.normal(ks[4], (L, 2 * D, D), dtype=jnp.float32) * s, 'b2': jnp.zeros((L, D), dtype=jnp.float32), 'We1': jax.random.normal(ks[5], (L, ED, D), dtype=jnp.float32) * s, 'be1': jnp.zeros((L, D), dtype=jnp.float32), 'We2': jax.random.normal(ks[6], (L, D, D), dtype=jnp.float32) * s, 'be2': jnp.zeros((L, D), dtype=jnp.float32), 'res_w': jnp.ones((L,), dtype=jnp.float32), 'dot_scale': jnp.ones((L,), dtype=jnp.float32), 'ln_g': jnp.ones((L, D), dtype=jnp.float32), 'ln_b': jnp.zeros((L, D), dtype=jnp.float32)}
    _L0_gnn_all = _L0_gnn_setup()
    _L0_gnn_in = {k: v for k, v in _L0_gnn_all.items() if k in ('W1', 'b1', 'W2', 'b2', 'We1', 'be1', 'We2', 'be2', 'res_w', 'dot_scale', 'ln_g', 'ln_b')}
    del _L0_gnn_all
    return {'x': x, 'src': src, 'dst': dst, 'edge_attr_32': edge_attr_32, 'L0_gnn_W1': _L0_gnn_in['W1'], 'L0_gnn_b1': _L0_gnn_in['b1'], 'L0_gnn_W2': _L0_gnn_in['W2'], 'L0_gnn_b2': _L0_gnn_in['b2'], 'L0_gnn_We1': _L0_gnn_in['We1'], 'L0_gnn_be1': _L0_gnn_in['be1'], 'L0_gnn_We2': _L0_gnn_in['We2'], 'L0_gnn_be2': _L0_gnn_in['be2'], 'L0_gnn_res_w': _L0_gnn_in['res_w'], 'L0_gnn_dot_scale': _L0_gnn_in['dot_scale'], 'L0_gnn_ln_g': _L0_gnn_in['ln_g'], 'L0_gnn_ln_b': _L0_gnn_in['ln_b']}

def reference(x, src, dst, edge_attr_32, L0_gnn_W1, L0_gnn_b1, L0_gnn_W2, L0_gnn_b2, L0_gnn_We1, L0_gnn_be1, L0_gnn_We2, L0_gnn_be2, L0_gnn_res_w, L0_gnn_dot_scale, L0_gnn_ln_g, L0_gnn_ln_b):
    import jax
    import jax.numpy as jnp

    def _L0_gnn_ref(x, edge_index, edge_attr, W1, b1, W2, b2, We1, be1, We2, be2, res_w, dot_scale, ln_g, ln_b):
        import jax, jax.numpy as jnp
        import numpy as np
        N, D, E, ED, L = (12500, 64, 100000, 32, 5)
        LN_EPS = 1e-05

        def _leaky(x):
            return jax.nn.leaky_relu(x, negative_slope=0.1)
        src, dst = (edge_index[0], edge_index[1])
        n = x.shape[0]
        for l in range(W1.shape[0]):
            h = _leaky(x @ W1[l] + b1[l]) @ W2[l] + b2[l]
            e = _leaky(edge_attr @ We1[l] + be1[l]) @ We2[l] + be2[l]
            msg = h[src] * e * dot_scale[l]
            agg = jax.ops.segment_sum(msg, dst, num_segments=n)
            out = x + agg * res_w[l]
            mu = jnp.mean(out, axis=-1, keepdims=True)
            var = jnp.mean(jnp.square(out - mu), axis=-1, keepdims=True)
            x = (out - mu) * jax.lax.rsqrt(var + LN_EPS) * ln_g[l] + ln_b[l]
        return x
    edge_index = jnp.stack([src, dst])
    h = jnp.maximum(_layernorm(x, axis=-1), 0.0)
    x = x + _L0_gnn_ref(h, edge_index, edge_attr_32, L0_gnn_W1, L0_gnn_b1, L0_gnn_W2, L0_gnn_b2, L0_gnn_We1, L0_gnn_be1, L0_gnn_We2, L0_gnn_be2, L0_gnn_res_w, L0_gnn_dot_scale, L0_gnn_ln_g, L0_gnn_ln_b)
    return x

_drawn_inputs = setup_inputs


def setup_inputs(seed=0):
    import zlib

    import numpy as np

    out = dict(_drawn_inputs(seed))
    spreads = {'L0_gnn_b1': (0.0, 0.1),
     'L0_gnn_b2': (0.0, 0.1),
     'L0_gnn_be1': (0.0, 0.1),
     'L0_gnn_be2': (0.0, 0.1),
     'L0_gnn_res_w': (1.0, 0.2),
     'L0_gnn_dot_scale': (1.0, 0.2),
     'L0_gnn_ln_g': (1.0, 0.2),
     'L0_gnn_ln_b': (0.0, 0.1)}
    factors = {}
    for name, (base, spread) in spreads.items():
        noise = np.random.default_rng([zlib.crc32(name.encode()), seed]).standard_normal(out[name].shape)
        drawn = base * np.exp(spread * noise) if base else spread * noise
        out[name] = jnp.asarray(drawn.astype(out[name].dtype))
    for name, factor in factors.items():
        out[name] = (out[name] * factor).astype(out[name].dtype)
    return out
```

```python
from contextlib import ExitStack

import concourse.bass as bass
from concourse import mybir

F32 = mybir.dt.float32
I32 = mybir.dt.int32
ALU = mybir.AluOpType
ACT = mybir.ActivationFunctionType

P = 128
TILE = 128
HALF = 512
GROUP = 1024
TPG = GROUP // TILE
TPH = HALF // TILE
RING = 4
WIN = 128
SUB = 4
TN = 448
ROWS = TN // SUB
SLOPE = 0.1
EPS = 1e-5


def sizes(n_nodes, n_edges):
    tiles = -(-n_nodes // (2 * TN))
    tiles += tiles % 2
    tiles = max(tiles, 4)
    groups = -(-n_edges // (GROUP * RING)) * RING
    return tiles, 2 * TN * tiles, groups


def build(nc, a, N, D, E, ED, L):
    NT, NPAD, NG = sizes(N, E)
    NHALF = NPAD // 2
    NPAIR = NT // 2
    IT = NG // RING
    H = 2 * D
    FW = NPAD // TN
    assert D == 64 and ED == 32 and IT > 1
    assert max(IT * L * 16 * TPG, NG * L * FW, NG * L * 32) < 2 ** 15

    h_rows = nc.dram_tensor("h_rows", (NPAD, D), F32, kind="Internal").ap()

    with ExitStack() as ctx:
        def sb(name, shape, dt=F32):
            return ctx.enter_context(nc.sbuf_tensor(name, shape, dt))

        def bank(name):
            return ctx.enter_context(nc.psum_tensor(name, [P, 512], F32))

        def sem(name):
            return ctx.enter_context(nc.semaphore(name))

        state = sb("state", [D, NPAD + WIN])
        x_packed = sb("x_packed", [P, NHALF])
        rel = sb("rel", [P, NG * TPG])
        far = sb("far", [P, NG * TPG])
        start_i = sb("start_i", [P, NG * 2], I32)
        column_i = sb("column_i", [P, TN], I32)
        column = sb("column", [P, TN])
        far_count = sb("far_count", [1, 1], I32)
        center = sb("center", [D, 3 * D])
        spread = sb("spread", [P, P])
        ones = sb("ones", [P, 1])
        eps = sb("eps", [P, 1])
        warm = sb("warm", [P, 1])
        far_sum = sb("far_sum", [P, 1])
        node_w = sb("node_w", [P, H + 2 * D + 1])
        ln_w = sb("ln_w", [P, 2])
        edge_w = sb("edge_w", [P, 2 * P + D + 3])
        scale = sb("scale", [P, 1])
        w2s = sb("w2s", [P, P])
        b2s = sb("b2s", [P, D])
        src = sb("src", [P, RING, TPG], I32)
        attr = sb("attr", [2 * ED, RING, HALF])
        rows = sb("rows", [P, RING, TPG * D])
        hid_sum = sb("hid_sum", [P, 2, HALF])
        hidden = sb("hidden", [P, 2, HALF])
        e_rows = sb("e_rows", [P, 2, TPG * D])
        pick = sb("pick", [P, 2, TPG, WIN])
        msg = sb("msg", [P, TPG * D])
        far_src = sb("far_src", [P, TPG], I32)
        far_attr = sb("far_attr", [2 * ED, HALF])
        far_rows = sb("far_rows", [P, TPG * D])
        far_rel = sb("far_rel", [P, TPG])
        far_pick = sb("far_pick", [P, TPG, TN])
        square = sb("square", [P, 2, TN])
        std = sb("std", [P, TN])
        rstd = sb("rstd", [P, TN])
        normed = sb("normed", [P, TN])
        y_sum = sb("y_sum", [P, 2, TN])
        y_act = sb("y_act", [P, 2, TN])
        h_out = sb("h_out", [ROWS, 2, 2 * SUB * D])
        final = sb("final", [P, 2, TN])

        banks = [bank(f"bank{i}") for i in range(8)]
        cent_ps = e_ps = banks[0:2]
        y_ps = hid_ps = banks[2:4]
        h_ps = banks[4:6]
        var_ps = far_ps = banks[6]
        win_ps = [banks[7], banks[4]]

        x_landed, state_landed, start_landed, dst_landed = (
            sem("x_landed"), sem("state_landed"), sem("start_landed"), sem("dst_landed"))
        filled, consts_ready, column_ready, eps_ready, table_ready = (
            sem("filled"), sem("consts_ready"), sem("column_ready"), sem("eps_ready"), sem("table_ready"))
        prep, counted, totalled, flag_ready = sem("prep"), sem("counted"), sem("totalled"), sem("flag_ready")
        node_w_landed, ln_landed, edge_w_landed = sem("node_w_landed"), sem("ln_landed"), sem("edge_w_landed")
        scale_ready, w2s_ready = sem("scale_ready"), sem("w2s_ready")
        hid_biased, far_hid_biased = sem("hid_biased"), sem("far_hid_biased")
        src_landed = [sem(f"src_landed{u}") for u in range(RING)]
        attr_landed = [sem(f"attr_landed{u}") for u in range(RING)]
        rows_landed = [sem(f"rows_landed{u}") for u in range(RING)]
        hid_ready, hid_acted, e_ready, e_biased, msg_ready, win_ready, added = (
            sem("hid_ready"), sem("hid_acted"), sem("e_ready"), sem("e_biased"), sem("msg_ready"),
            sem("win_ready"), sem("added"))
        far_src_landed, far_attr_landed = sem("far_src_landed"), sem("far_attr_landed")
        far_rows_landed = [sem(f"far_rows_landed{u}") for u in range(4)]
        far_hid_ready, far_hid_acted, far_e_ready, far_e_biased = (
            sem("far_hid_ready"), sem("far_hid_acted"), sem("far_e_ready"), sem("far_e_biased"))
        far_rel_ready, far_picked, far_win_ready, far_added = (
            sem("far_rel_ready"), sem("far_picked"), sem("far_win_ready"), sem("far_added"))
        cent_ready, square_ready, var_ready, std_ready, rstd_ready, norm_ready, low_ready, high_ready = (
            sem("cent_ready"), sem("square_ready"), sem("var_ready"), sem("std_ready"),
            sem("rstd_ready"), sem("norm_ready"), sem("low_ready"), sem("high_ready"))
        y_biased = sem("y_biased")
        y_ready, y_acted, h_ready, h_biased = sem("y_ready"), sem("y_acted"), sem("h_ready"), sem("h_biased")
        h_stored = [sem(f"h_stored{u}") for u in range(2)]
        affine_ready, final_ready = sem("affine_ready"), sem("final_ready")
        out_stored = [sem(f"out_stored{u}") for u in range(2)]

        passed = {e: sem(f"passed_{e}") for e in ("sp", "pool", "pe", "dve")}

        block = ctx.enter_context(nc.Block())
        ds = bass.ds

        NC = NG * TPG
        assert 2 * NC + 2 * NG <= TPG * TN
        far_pick_flat = far_pick[:, :, :].rearrange("p t w -> p (t w)")

        def scratch(n):
            return far_pick_flat[:, n * NC:(n + 1) * NC]

        def own_wait(eng, name):
            eng.sem_inc(passed[name], 1)

        def low(t):
            return state[:, ds(t * TN, TN)]

        def high(t):
            return state[:, ds(t * TN + NHALF, TN)]

        def one(table, n):
            return table[ds(n, 1)].rearrange("a p c -> (a p) c")

        def rounds(eng, node, edges, last):
            node(0, True)
            if L > 1:
                with eng.Fori(0, L - 1) as l:
                    edges(l, False)
                    node(l + 1, False)
            edges(L - 1, True)
            last()

        def node_tiles(eng, norm, both, mlp):
            norm(0, 0)
            for j in range(2):
                both(j, j, None)
            if NPAIR > 2:
                with eng.Fori(1, NPAIR - 1) as i:
                    for j in range(2):
                        both(2 * i + j, j, i)
            both(NT - 2, 0, NPAIR - 1)
            mlp(NT - 1, 1, NPAIR - 1)

        def edge_groups(eng, group):
            with eng.Fori(0, IT - 1) as i:
                for u in range(RING):
                    group(i, u, 2)
            for u in range(RING):
                group(IT - 1, u, min(2, RING - 1 - u))

        def if_far(eng, body):
            eng.wait_ge(flag_ready, 1)
            count = eng.value_load(far_count[0:1, 0:1], min_val=0, max_val=NG * GROUP)
            with eng.If(count > 0):
                body()

        @block.sync
        def _(sp):
            sp.dma_start(state[:, 0:NPAD], a["x_t"]).then_inc(state_landed, 16)
            sp.dma_start(node_w[:, :], one(a["node_pack"], 0)).then_inc(node_w_landed, 16)
            sp.dma_start(edge_w[:, :], one(a["edge_pack"], 0)).then_inc(edge_w_landed, 16)
            sp.dma_start(start_i[:, :], a["starts"].to_broadcast((P, 2 * NG))).then_inc(start_landed, 16)
            sp.dma_start(scratch(0).bitcast(I32), a["dst_tiles"]).then_inc(dst_landed, 16)

            def load(g, u):
                sp.dma_start(src[:, u, :], one(a["src_tiles"], g)).then_inc(src_landed[u], 16)
                sp.dma_start(attr[:, u, :], one(a["attr_t"], g)).then_inc(attr_landed[u], 16)

            for u in range(RING):
                load(u, u)
            sp.dma_start(x_packed[0:D, :], a["x_t"][:, 0:NHALF]).then_inc(x_landed, 16)
            sp.dma_start(x_packed[D:P, :], a["x_t"][:, NHALF:NPAD]).then_inc(x_landed, 16)

            def node(k, first):
                with sp.Fori(0, NPAIR) as i:
                    for j in range(2):
                        t = 2 * i + j
                        sp.wait_ge(h_biased, k * NT + t + 1)
                        for side in range(2):
                            to = h_rows[ds(t * TN + side * NHALF, TN), :]
                            sp.dma_start(to.rearrange("(p s) f -> p (s f)", s=SUB),
                                         h_out[:, j, side * SUB * D:(side + 1) * SUB * D]
                                         ).then_inc(h_stored[j], 16)

            def far_pass(l):
                with sp.Fori(0, NG) as g:
                    sp.wait_ge(far_added, (l * NG + g) * FW + 1)
                    sp.dma_start(far_src[:, :], one(a["src_tiles"], g)).then_inc(far_src_landed, 16)
                    sp.dma_start(far_attr[:, :], one(a["attr_t"], g)).then_inc(far_attr_landed, 16)
                sp.wait_ge(far_added, (l + 1) * NG * FW + 1)
                own_wait(sp, "sp")

            def edges(l, last):
                sp.dma_start(ln_w[:, :], one(a["ln_pack"], l)).then_inc(ln_landed, 16)
                if not last:
                    sp.dma_start(node_w[:, :], one(a["node_pack"], l + 1)).then_inc(node_w_landed, 16)
                with sp.Fori(0, IT - 1) as i:
                    for u in range(RING):
                        sp.wait_ge(msg_ready, l * NG + i * RING + u + 1)
                        load(i * RING + RING + u, u)
                if not last:
                    for u in range(RING):
                        sp.wait_ge(msg_ready, l * NG + NG - RING + u + 1)
                        load(u, u)
                    sp.wait_ge(added, 2 * NG * (l + 1) + 1)
                    own_wait(sp, "sp")
                if_far(sp, lambda: far_pass(l))
                if not last:
                    sp.dma_start(edge_w[:, :], one(a["edge_pack"], l + 1)).then_inc(edge_w_landed, 16)

            def last():
                with sp.Fori(0, NPAIR) as i:
                    for j in range(2):
                        sp.wait_ge(final_ready, 2 * i + j + 1)
                        sp.dma_start(a["y"][:, ds((2 * i + j) * TN, TN)], final[:, j, :]
                                     ).then_inc(out_stored[j], 16)

            rounds(sp, node, edges, last)
            for j in range(2):
                sp.wait_ge(out_stored[j], 16 * NPAIR)

        @block.gpsimd
        def _(pool):
            pool.iota(column_i[:, :], pattern=[[1, TN]], base=0, channel_multiplier=0).then_inc(column_ready, 1)
            pool.wait_ge(filled, 7)
            for c in (0, 2):
                part = center[:, c * D:(c + 1) * D]
                pool.affine_select(out=part, in_=part, compare_op=ALU.not_equal, fill=1.0 - 1.0 / D,
                                   base=0, pattern=[[-1, D]], channel_multiplier=1).then_inc(consts_ready, 1)

            def gathers(index, to, landed):
                for j in range(TPH):
                    for side in range(2):
                        t, at = side * TPH + j, (2 * j + side) * D
                        pool.indirect_dma_start(
                            to[:, at:at + D], None, h_rows,
                            bass.IndirectOffsetOnAxis(ap=index[:, t:t + 1], axis=0)).then_inc(landed(t), 16)

            def far_pass(l):
                with pool.Fori(0, NG) as g:
                    pool.wait_ge(far_src_landed, 16 * (l * NG + g + 1))
                    own_wait(pool, "pool")
                    gathers(far_src, far_rows, lambda t: far_rows_landed[t % 4])

            def edges(l, last):
                for j in range(2):
                    pool.wait_ge(h_stored[j], 32 * NPAIR * (l + 1))
                    own_wait(pool, "pool")

                def group(i, u, after):
                    pool.wait_ge(src_landed[u], 16 * (l * IT + i + 1))
                    own_wait(pool, "pool")
                    gathers(src[:, u, :], rows[:, u, :], lambda t: rows_landed[u])

                edge_groups(pool, group)
                if_far(pool, lambda: far_pass(l))

            rounds(pool, lambda k, first: None, edges, lambda: None)

        @block.tensor
        def _(pe):
            def centered(t, j):
                pe.matmul(cent_ps[j][:, 0:TN], center[:, 0:P], low(t), start=True, stop=False)
                pe.matmul(cent_ps[j][:, 0:TN], center[:, D:3 * D], high(t), start=False, stop=True
                          ).then_inc(cent_ready, 1)

            def variance(q, j):
                pe.wait_ge(square_ready, q + 1)
                pe.matmul(var_ps[:, 0:TN], spread[:, :], square[:, j, :], start=True, stop=True
                          ).then_inc(var_ready, 1)

            def node(k, first):
                if first:
                    pe.wait_ge(consts_ready, 2)
                    pe.wait_ge(state_landed, 16)
                pe.wait_ge(node_w_landed, 16 * (k + 1))

                def norm(t, j):
                    centered(t, j)
                    variance(k * NT + t, j)

                def y(q, t):
                    pe.wait_ge(low_ready, q + 1)
                    own_wait(pe, "pe")
                    pe.matmul(y_ps[0][:, 0:TN], node_w[0:D, 0:H], low(t), start=True, stop=True).then_inc(y_ready, 1)
                    pe.wait_ge(high_ready, q + 1)
                    own_wait(pe, "pe")
                    pe.matmul(y_ps[1][:, 0:TN], node_w[0:D, 0:H], high(t), start=True, stop=True).then_inc(y_ready, 1)

                def h(q, j):
                    for side in range(2):
                        pe.wait_ge(y_acted, 2 * q + side + 1)
                        for s in range(SUB):
                            at = (side * SUB + s) * D
                            mm = pe.matmul(h_ps[j][0:ROWS, at:at + D], y_act[:, side, s:TN:SUB],
                                           node_w[:, H:H + D], start=True, stop=True)
                    mm.then_inc(h_ready, 1)

                def both(t, j, i):
                    centered(t + 1, 1 - j)
                    y(k * NT + t, t)
                    variance(k * NT + t + 1, 1 - j)
                    h(k * NT + t, j)

                def mlp(t, j, i):
                    y(k * NT + t, t)
                    h(k * NT + t, j)

                node_tiles(pe, norm, both, mlp)
                if first:
                    pe.wait_ge(counted, 1)
                    pe.matmul(win_ps[0][0:1, 0:1], far_sum[:, :], ones[:, :], start=True, stop=True
                              ).then_inc(totalled, 1)

            def edge_hidden(attributes, v):
                return pe.matmul(hid_ps[v][:, :], edge_w[0:2 * ED, 0:P], attributes, start=True, stop=True)

            def edge_out(v):
                for j in range(TPH):
                    mm = pe.matmul(e_ps[v][:, j * P:(j + 1) * P], hidden[:, v, j * TILE:(j + 1) * TILE],
                                   w2s[:, :], start=True, stop=True)
                return mm

            def far_pass(l):
                with pe.Fori(0, NG) as g:
                    n = l * NG + g
                    pe.wait_ge(far_attr_landed, 16 * (n + 1))
                    edge_hidden(far_attr[:, :], 0).then_inc(far_hid_ready, 1)
                    pe.wait_ge(far_hid_acted, n + 1)
                    edge_out(0).then_inc(far_e_ready, 1)
                    with pe.Fori(0, FW) as w:
                        pe.wait_ge(far_picked, n * FW + w + 1)
                        for t in range(TPG):
                            at = (2 * (t % TPH) + t // TPH) * D
                            mm = pe.matmul(far_ps[0:D, 0:TN], msg[:, at:at + D], far_pick[:, t, :],
                                           start=(t == 0), stop=(t == TPG - 1))
                        mm.then_inc(far_win_ready, 1)
                pe.wait_ge(far_added, (l + 1) * NG * FW + 1)
                own_wait(pe, "pe")

            def edges(l, last):
                pe.wait_ge(edge_w_landed, 16 * (l + 1))
                pe.wait_ge(w2s_ready, 2 * (l + 1))
                pe.wait_ge(h_biased, (l + 1) * NT)
                own_wait(pe, "pe")

                def hidden_of(u, use):
                    pe.wait_ge(attr_landed[u], 16 * (l * IT + use + 1))
                    edge_hidden(attr[:, u, :], u % 2).then_inc(hid_ready, 1)

                def out_of(n, v):
                    pe.wait_ge(hid_acted, n + 1)
                    edge_out(v).then_inc(e_ready, 1)

                hidden_of(0, 0)
                hidden_of(1, 0)
                out_of(l * NG, 0)

                def group(i, u, after):
                    n, v = l * NG + i * RING + u, u % 2
                    if after > 1:
                        hidden_of((u + 2) % RING, i + (u + 2) // RING)
                    if after > 0:
                        out_of(n + 1, 1 - v)
                    pe.wait_ge(msg_ready, n + 1)
                    for side in range(2):
                        for j in range(TPH):
                            at = (2 * j + side) * D
                            mm = pe.matmul(win_ps[side][0:D, 0:WIN], msg[:, at:at + D],
                                           pick[:, v, side * TPH + j, :], start=(j == 0), stop=(j == TPH - 1))
                        mm.then_inc(win_ready, 1)

                edge_groups(pe, group)
                pe.wait_ge(added, 2 * NG * (l + 1) + 1)
                own_wait(pe, "pe")
                if_far(pe, lambda: far_pass(l))

            def last():
                def both(t, j, i):
                    if i is not None or j:
                        pe.wait_ge(norm_ready, L * NT + t)
                        own_wait(pe, "pe")
                    centered(t + 1, 1 - j)
                    variance(L * NT + t, j)

                def tail(t, j, i):
                    pe.wait_ge(norm_ready, L * NT + t)
                    variance(L * NT + t, j)

                node_tiles(pe, centered, both, tail)

            rounds(pe, node, edges, last)

        @block.scalar
        def _(act):
            act.wait_ge(eps_ready, 1)
            act.activation(warm[:, :], eps[:, :], ACT.Sqrt).then_inc(table_ready, 1)

            def squared(q, j):
                act.wait_ge(cent_ready, q + 1)
                act.activation(square[:, j, :], cent_ps[j][:, 0:TN], ACT.Square).then_inc(square_ready, 1)

            def root(q):
                act.wait_ge(var_ready, q + 1)
                act.activation(std[:, :], var_ps[:, 0:TN], ACT.Sqrt, bias=eps[:, :]).then_inc(std_ready, 1)

            def node(k, first):
                if not first:
                    act.wait_ge(ln_landed, 16 * k)

                def affine(q, t):
                    act.wait_ge(norm_ready, q + 1)
                    if first:
                        act.activation(high(t), normed[D:P, :], ACT.Relu).then_inc(high_ready, 1)
                    else:
                        act.activation(high(t), normed[D:P, :], ACT.Identity, scale=ln_w[D:P, 0:1],
                                       bias=ln_w[D:P, 1:2]).then_inc(high_ready, 1)

                def biased(q):
                    for side in range(2):
                        act.wait_ge(y_ready, 2 * q + side + 1)
                        act.activation(y_sum[:, side, :], y_ps[side][:, 0:TN], ACT.Identity,
                                       bias=node_w[:, H + 2 * D:H + 2 * D + 1]).then_inc(y_biased, 1)

                def norm(t, j):
                    squared(k * NT + t, j)
                    root(k * NT + t)
                    affine(k * NT + t, t)

                def both(t, j, i):
                    squared(k * NT + t + 1, 1 - j)
                    biased(k * NT + t)
                    root(k * NT + t + 1)
                    affine(k * NT + t + 1, t + 1)

                node_tiles(act, norm, both, lambda t, j, i: biased(k * NT + t))

            def hidden_biased(v):
                return act.activation(hid_sum[:, v, :], hid_ps[v][:, :], ACT.Identity,
                                      bias=edge_w[:, 2 * P + D:2 * P + D + 1])

            def far_pass(l):
                with act.Fori(0, NG) as g:
                    act.wait_ge(far_hid_ready, l * NG + g + 1)
                    hidden_biased(0).then_inc(far_hid_biased, 1)

            def edges(l, last):
                def group(i, u, after):
                    act.wait_ge(hid_ready, l * NG + i * RING + u + 1)
                    hidden_biased(u % 2).then_inc(hid_biased, 1)

                edge_groups(act, group)
                if_far(act, lambda: far_pass(l))

            def last():
                act.wait_ge(ln_landed, 16 * L)

                def scaled(t, j, i):
                    q = L * NT + t
                    root(q)
                    act.wait_ge(norm_ready, q + 1)
                    if i is not None:
                        act.wait_ge(out_stored[j], 16 * i)
                    act.activation(final[:, j, :], normed[:, :], ACT.Identity, scale=ln_w[:, 0:1],
                                   bias=ln_w[:, 1:2]).then_inc(affine_ready, 1)

                def both(t, j, i):
                    squared(L * NT + t + 1, 1 - j)
                    scaled(t, j, i)

                node_tiles(act, lambda t, j: squared(L * NT + t, j), both, scaled)

            rounds(act, node, edges, last)

        @block.vector
        def _(dve):
            dve.memset(eps[:, :], EPS).then_inc(eps_ready, 1)
            dve.memset(state[:, NPAD:NPAD + WIN], 0.0).then_inc(added, 1)
            dve.memset(ones[:, :], 1.0).then_inc(far_added, 1)
            dve.memset(center[:, D:2 * D], 0.0).then_inc(filled, 1)
            for c in (0, 2):
                dve.memset(center[:, c * D:(c + 1) * D], -1.0 / D).then_inc(filled, 1)
            for r in range(2):
                for c in range(2):
                    dve.memset(spread[r * D:(r + 1) * D, c * D:(c + 1) * D], 1.0 / D if r == c else 0.0
                                ).then_inc(filled, 1)
            dve.wait_ge(column_ready, 1)
            dve.tensor_copy(column[:, :], column_i[:, :]).then_inc(column_ready, 1)

            def place_edges():
                inside, upper, start_f = scratch(0), scratch(1), far_pick_flat[:, 2 * NC:2 * NC + 2 * NG]

                def prepared(instruction, n):
                    instruction.then_inc(prep, 1)
                    dve.wait_ge(prep, n)

                dve.wait_ge(dst_landed, 16)
                prepared(dve.tensor_copy(far[:, :], scratch(0).bitcast(I32)), 1)
                dve.wait_ge(start_landed, 16)
                prepared(dve.tensor_copy(start_f, start_i[:, :]), 2)
                prepared(dve.tensor_tensor(rel[:, :].rearrange("p (h j) -> p h j", j=TPH),
                                           far[:, :].rearrange("p (h j) -> p h j", j=TPH),
                                           start_f.unsqueeze(2).to_broadcast((P, 2 * NG, TPH)), ALU.subtract), 3)
                prepared(dve.tensor_single_scalar(inside, rel[:, :], 0.0, ALU.is_ge), 4)
                prepared(dve.scalar_tensor_tensor(upper, rel[:, :], float(WIN), inside, ALU.is_lt, ALU.mult), 5)
                prepared(dve.scalar_tensor_tensor(inside, far[:, :], 1.0, upper, ALU.add, ALU.mult), 6)
                prepared(dve.tensor_tensor(far[:, :], far[:, :], inside, ALU.subtract), 7)
                prepared(dve.tensor_single_scalar(inside, far[:, :], 0.0, ALU.is_ge), 8)
                prepared(dve.scalar_tensor_tensor(upper, far[:, :], float(N), inside, ALU.is_lt, ALU.mult), 9)
                dve.reduce_sum(far_sum[:, :], upper, axis=mybir.AxisListType.X).then_inc(counted, 1)
                dve.wait_ge(totalled, 1)
                dve.tensor_copy(far_count[:, :], win_ps[0][0:1, 0:1]).then_inc(flag_ready, 1)

            def leaky(out, y):
                return dve.scalar_tensor_tensor(out, y, SLOPE, y, ALU.mult, ALU.max)

            def normalize(q, j):
                dve.wait_ge(std_ready, q + 1)
                dve.reciprocal(rstd[:, :], std[:, :]).then_inc(rstd_ready, 1)
                dve.wait_ge(rstd_ready, q + 1)
                dve.tensor_tensor(normed[:, :], cent_ps[j][:, 0:TN], rstd[:, :], ALU.mult).then_inc(norm_ready, 1)

            def node(k, first):
                if not first:
                    dve.wait_ge(ln_landed, 16 * k)

                def norm(t, j):
                    q = k * NT + t
                    normalize(q, j)
                    dve.wait_ge(norm_ready, q + 1)
                    if first:
                        dve.tensor_single_scalar(low(t), normed[0:D, :], 0.0, ALU.max).then_inc(low_ready, 1)
                    else:
                        dve.tensor_scalar(low(t), normed[0:D, :], ln_w[0:D, 0:1], ln_w[0:D, 1:2],
                                          ALU.mult, ALU.add).then_inc(low_ready, 1)

                def biased(t, j, i):
                    dve.wait_ge(h_ready, k * NT + t + 1)
                    if i is not None:
                        dve.wait_ge(h_stored[j], 32 * (k * NPAIR + i))
                    dve.tensor_tensor(h_out[:, j, :].rearrange("p (s f) -> p s f", f=D),
                                      h_ps[j][0:ROWS, :].rearrange("p (s f) -> p s f", f=D),
                                      node_w[0:ROWS, H + D:H + 2 * D].unsqueeze(1).to_broadcast((ROWS, 2 * SUB, D)),
                                      ALU.add).then_inc(h_biased, 1)

                def acted(t):
                    for side in range(2):
                        dve.wait_ge(y_biased, 2 * (k * NT + t) + side + 1)
                        leaky(y_act[:, side, :], y_sum[:, side, :]).then_inc(y_acted, 1)

                def both(t, j, i):
                    acted(t)
                    norm(t + 1, 1 - j)
                    biased(t, j, i)

                def mlp(t, j, i):
                    acted(t)
                    biased(t, j, i)

                node_tiles(dve, norm, both, mlp)
                if first:
                    place_edges()

            def edge_biased(v):
                return dve.tensor_tensor(e_rows[:, v, :].rearrange("p (t f) -> p t f", f=D),
                                         e_ps[v][:, :].rearrange("p (t f) -> p t f", f=D),
                                         b2s[:, :].unsqueeze(1).to_broadcast((P, TPG, D)), ALU.add)

            def one_hot(out, width, where):
                return dve.tensor_tensor(out, column[:, 0:width].unsqueeze(1).to_broadcast((P, TPG, width)),
                                         where.unsqueeze(2).to_broadcast((P, TPG, width)), ALU.is_equal)

            def far_pass(l):
                with dve.Fori(0, NG) as g:
                    n = l * NG + g
                    dve.tensor_copy(far_rel[:, :], far[:, ds(g * TPG, TPG)]).then_inc(far_rel_ready, 1)
                    dve.wait_ge(far_hid_biased, n + 1)
                    leaky(hidden[:, 0, :], hid_sum[:, 0, :]).then_inc(far_hid_acted, 1)
                    dve.wait_ge(far_e_ready, n + 1)
                    edge_biased(0).then_inc(far_e_biased, 1)
                    dve.wait_ge(far_e_biased, n + 1)
                    for t in range(4):
                        dve.wait_ge(far_rows_landed[t], 32 * (n + 1))
                    dve.tensor_tensor(msg[:, :], far_rows[:, :], e_rows[:, 0, :], ALU.mult)
                    with dve.Fori(0, FW) as w:
                        m = n * FW + w
                        dve.wait_ge(far_rel_ready, n * (FW + 1) + w + 1)
                        one_hot(far_pick[:, :, :], TN, far_rel[:, :]).then_inc(far_picked, 1)
                        dve.wait_ge(far_picked, m + 1)
                        dve.tensor_scalar_add(far_rel[:, :], far_rel[:, :], -float(TN)).then_inc(far_rel_ready, 1)
                        dve.wait_ge(far_win_ready, m + 1)
                        dve.wait_ge(far_added, m + 1)
                        dve.tensor_tensor(state[:, ds(w * TN, TN)], state[:, ds(w * TN, TN)],
                                          far_ps[0:D, 0:TN], ALU.add).then_inc(far_added, 1)
                    dve.wait_ge(far_rel_ready, (n + 1) * (FW + 1))
                    own_wait(dve, "dve")

            def edges(l, last):
                dve.wait_ge(edge_w_landed, 16 * (l + 1))
                dve.tensor_tensor(scale[:, :], edge_w[:, 2 * P + D + 1:2 * P + D + 2],
                                  edge_w[:, 2 * P + D + 2:2 * P + D + 3], ALU.mult).then_inc(scale_ready, 1)
                dve.wait_ge(scale_ready, l + 1)
                dve.tensor_scalar_mul(w2s[:, :], edge_w[:, P:2 * P], scale[:, :]).then_inc(w2s_ready, 1)
                dve.tensor_scalar_mul(b2s[:, :], edge_w[:, 2 * P:2 * P + D], scale[:, :]).then_inc(w2s_ready, 1)
                dve.wait_ge(w2s_ready, 2 * (l + 1))
                own_wait(dve, "dve")
                def acted(n, v):
                    dve.wait_ge(hid_biased, n + 1)
                    leaky(hidden[:, v, :], hid_sum[:, v, :]).then_inc(hid_acted, 1)

                def out_biased(n, v):
                    dve.wait_ge(e_ready, n + 1)
                    edge_biased(v).then_inc(e_biased, 1)

                def picked(g, v):
                    one_hot(pick[:, v, :, :], WIN, rel[:, ds(g * TPG, TPG)])

                acted(l * NG, 0)
                acted(l * NG + 1, 1)
                out_biased(l * NG, 0)
                picked(0, 0)

                def group(i, u, after):
                    g, v = i * RING + u, u % 2
                    n = l * NG + g
                    starts = [dve.value_load(start_i[0:1, ds(2 * g + side, 1)], min_val=0, max_val=NPAD)
                              for side in range(2)]
                    if after > 1:
                        acted(n + 2, v)
                    if after > 0:
                        out_biased(n + 1, 1 - v)
                    dve.wait_ge(e_biased, n + 1)
                    dve.wait_ge(rows_landed[u], 16 * TPG * (l * IT + i + 1))
                    dve.tensor_tensor(msg[:, :], rows[:, u, :], e_rows[:, v, :], ALU.mult).then_inc(msg_ready, 1)
                    if after > 0:
                        picked(g + 1, 1 - v)
                    for side in range(2):
                        dve.wait_ge(win_ready, 2 * n + side + 1)
                        dve.wait_ge(added, 2 * n + side + 1)
                        window = state[:, ds(starts[side], WIN)]
                        dve.tensor_tensor(window, window, win_ps[side][0:D, 0:WIN],
                                          ALU.add).then_inc(added, 1)

                edge_groups(dve, group)
                if_far(dve, lambda: far_pass(l))

            def last():
                dve.wait_ge(x_landed, 32)

                def tile(t, j, i):
                    normalize(L * NT + t, j)
                    dve.wait_ge(affine_ready, t + 1)
                    dve.tensor_tensor(final[:, j, :], final[:, j, :], x_packed[:, ds(t * TN, TN)],
                                      ALU.add).then_inc(final_ready, 1)

                node_tiles(dve, lambda t, j: None, tile, tile)

            dve.wait_ge(column_ready, 2)
            rounds(dve, node, edges, last)

    return nc


def kernel(x, src, dst, edge_attr_32, L0_gnn_W1, L0_gnn_b1, L0_gnn_W2, L0_gnn_b2, L0_gnn_We1, L0_gnn_be1,
           L0_gnn_We2, L0_gnn_be2, L0_gnn_res_w, L0_gnn_dot_scale, L0_gnn_ln_g, L0_gnn_ln_b):
    import numpy as np
    import concourse.bacc as bacc
    from concourse.bass_utils import run_bass_kernel_spmd

    x, src, dst, attr, W1, b1, W2, b2, We1, be1, We2, be2, res, dot, g, b = (
        np.asarray(v) for v in (x, src, dst, edge_attr_32, L0_gnn_W1, L0_gnn_b1, L0_gnn_W2, L0_gnn_b2,
                                L0_gnn_We1, L0_gnn_be1, L0_gnn_We2, L0_gnn_be2, L0_gnn_res_w,
                                L0_gnn_dot_scale, L0_gnn_ln_g, L0_gnn_ln_b))
    (N, D), (E, ED), L = x.shape, attr.shape, W1.shape[0]
    NT, NPAD, NG = sizes(N, E)
    pad = NG * GROUP - E

    x_t = np.ascontiguousarray(np.pad(x, ((0, NPAD - N), (0, 0))).T)
    src_tiles = np.ascontiguousarray(np.pad(src, (0, pad)).reshape(NG, TPG, TILE).transpose(0, 2, 1))
    dst_all = np.pad(dst, (0, pad), constant_values=NPAD)
    dst_tiles = np.ascontiguousarray(dst_all.reshape(NG * TPG, TILE).T)
    starts = np.ascontiguousarray(dst_all.reshape(NG * 2, HALF)[:, 0][None, :])
    attr_t = np.ascontiguousarray(
        np.pad(attr, ((0, pad), (0, 0))).reshape(NG, 2, HALF, ED).transpose(0, 1, 3, 2).reshape(NG, 2 * ED, HALF))

    def on_rows(v):
        return np.broadcast_to(v[:, None, :], (L, P, v.shape[1]))

    def down(v):
        return np.concatenate([v, v], 1)[:, :, None]

    w1 = np.concatenate([W1, np.zeros_like(W1)], 1)
    node_pack = np.ascontiguousarray(np.concatenate([w1, W2, on_rows(b2), b1[:, :, None]], 2))
    we1 = np.zeros((L, P, P), x.dtype)
    we1[:, 0:ED, 0:D] = We1
    we1[:, ED:2 * ED, D:P] = We1
    we2 = np.zeros((L, P, P), x.dtype)
    we2[:, 0:D, 0:D] = We2
    we2[:, D:P, D:P] = We2
    edge_pack = np.ascontiguousarray(np.concatenate(
        [we1, we2, on_rows(be2), down(be1), on_rows(dot[:, None]), on_rows(res[:, None])], 2))
    ln_pack = np.ascontiguousarray(np.concatenate([down(g), down(b)], 2))

    arrays = dict(x_t=x_t, src_tiles=src_tiles, dst_tiles=dst_tiles, starts=starts, attr_t=attr_t,
                  node_pack=node_pack, edge_pack=edge_pack, ln_pack=ln_pack)
    nc = bacc.Bacc("TRN2", target_bir_lowering=False, num_devices=1)
    aps = {n: nc.dram_tensor(n, v.shape, mybir.dt.from_np(v.dtype), kind="ExternalInput").ap()
           for n, v in arrays.items()}
    aps["y"] = nc.dram_tensor("y", (P, NPAD // 2), F32, kind="ExternalOutput").ap()
    build(nc, aps, N, D, E, ED, L)
    y = run_bass_kernel_spmd(nc, [arrays], core_ids=[0]).results[0]["y"]
    return np.ascontiguousarray(y.reshape(2, D, NPAD // 2).transpose(0, 2, 1).reshape(NPAD, D)[0:N])
```

```python
from contextlib import ExitStack

import concourse.bass as bass
from concourse import mybir

F32 = mybir.dt.float32
I32 = mybir.dt.int32
ALU = mybir.AluOpType
ACT = mybir.ActivationFunctionType

P = 128
TILE = 128
HALF = 512
GROUP = 1024
TPG = GROUP // TILE
TPH = HALF // TILE
RING = 4
WIN = 128
SUB = 4
TN = 448
ROWS = TN // SUB
SLOPE = 0.1
EPS = 1e-5


def sizes(n_nodes, n_edges):
    tiles = -(-n_nodes // (2 * TN))
    tiles += tiles % 2
    tiles = max(tiles, 4)
    groups = -(-n_edges // (GROUP * RING)) * RING
    return tiles, 2 * TN * tiles, groups


def build(nc, a, N, D, E, ED, L):
    NT, NPAD, NG = sizes(N, E)
    NHALF = NPAD // 2
    NPAIR = NT // 2
    IT = NG // RING
    H = 2 * D
    FW = NPAD // TN
    NC = NG * TPG
    last_tiles = [max(0, min(TPG, -(-E // TILE) - (NG - RING + u) * TPG)) for u in range(RING)]
    rows_of_round = [16 * (TPG * (IT - 1) + tiles) for tiles in last_tiles]
    assert D == 64 and ED == 32 and IT > 1
    assert max(IT * L * 16 * TPG, NG * L * FW, NG * L * 32) < 2 ** 15

    assert 2 * NG <= TN and NT <= 32

    h_rows = [nc.dram_tensor(f"h_rows{p}", (NPAD, D), F32, kind="Internal").ap() for p in range(2)]

    with ExitStack() as ctx:
        def sb(name, shape, dt=F32):
            return ctx.enter_context(nc.sbuf_tensor(name, shape, dt))

        def bank(name):
            return ctx.enter_context(nc.psum_tensor(name, [P, 512], F32))

        def sem(name):
            return ctx.enter_context(nc.semaphore(name))

        state = sb("state", [D, NPAD + WIN])
        x_packed = sb("x_packed", [P, NHALF])
        rel = sb("rel", [P, NG * TPG])
        far = sb("far", [P, NG * TPG])
        start_i = sb("start_i", [P, NG * 2], I32)
        column_i = sb("column_i", [P, TN], I32)
        column = sb("column", [P, TN])
        far_count = sb("far_count", [1, 1], I32)
        center = sb("center", [D, 3 * D])
        center_both = sb("center_both", [P, P])
        spread = sb("spread", [P, P])
        ones = sb("ones", [P, NT])
        part_i = sb("part_i", [P, 1], I32)
        part = sb("part", [P, 1])
        plan = sb("plan", [NT, 3, TN])
        due = sb("due", [NT, 6])
        tile_go = sb("tile_go", [1, IT], I32)
        tile_at = sb("tile_at", [1, IT], I32)
        tiles_in_loop = sb("tiles_in_loop", [1, 1], I32)
        eps = sb("eps", [P, 1])
        warm = sb("warm", [P, 1])
        far_sum = sb("far_sum", [P, 1])
        node_w = sb("node_w", [P, H + 2 * D + 1])
        ln_w = sb("ln_w", [P, 2])
        edge_w = sb("edge_w", [P, 2 * P + D + 3])
        scale = sb("scale", [P, 1])
        w2s = sb("w2s", [P, P])
        b2s = sb("b2s", [P, D])
        src = sb("src", [P, RING, TPG], I32)
        attr = sb("attr", [2 * ED, RING, HALF])
        rows = sb("rows", [P, RING, TPG * D])
        hid_sum = sb("hid_sum", [P, 2, HALF])
        hidden = sb("hidden", [P, 2, HALF])
        e_rows = sb("e_rows", [P, 2, TPG * D])
        pick = sb("pick", [P, 2, TPG, WIN])
        msg = sb("msg", [P, TPG * D])
        far_src = sb("far_src", [P, TPG], I32)
        far_attr = sb("far_attr", [2 * ED, HALF])
        far_rows = sb("far_rows", [P, TPG * D])
        far_rel = sb("far_rel", [P, TPG])
        far_pick = sb("far_pick", [P, TPG, TN])
        square = sb("square", [P, 2, TN])
        std = sb("std", [P, TN])
        rstd = sb("rstd", [P, TN])
        normed = sb("normed", [P, TN])
        y_sum = sb("y_sum", [P, 2, TN])
        y_act = sb("y_act", [P, 2, TN])
        h_out = sb("h_out", [ROWS, 2 * SUB * D])
        final = sb("final", [P, TN])

        banks = [bank(f"bank{i}") for i in range(8)]
        cent_ps = e_ps = banks[0:2]
        y_ps = hid_ps = banks[2:4]
        h_ps = banks[4:6]
        var_ps = far_ps = banks[6]
        win_ps = [banks[7], banks[4]]
        tile_ps = [banks[5], banks[6]]

        x_head_landed, start_landed, dst_landed = sem("x_head_landed"), sem("start_landed"), sem("dst_landed")
        planned, plan_product, plan_ready = sem("planned"), sem("plan_product"), sem("plan_ready")
        filled, consts_ready, column_ready, eps_ready, table_ready = (
            sem("filled"), sem("consts_ready"), sem("column_ready"), sem("eps_ready"), sem("table_ready"))
        prep, counted, totalled, flag_ready = sem("prep"), sem("counted"), sem("totalled"), sem("flag_ready")
        node_w_landed, ln_landed, edge_w_landed = sem("node_w_landed"), sem("ln_landed"), sem("edge_w_landed")
        scale_ready, w2s_ready = sem("scale_ready"), sem("w2s_ready")
        hid_biased, far_hid_biased = sem("hid_biased"), sem("far_hid_biased")
        src_landed = [sem(f"src_landed{u}") for u in range(RING)]
        attr_landed = [sem(f"attr_landed{u}") for u in range(RING)]
        rows_landed = [sem(f"rows_landed{u}") for u in range(RING)]
        hid_ready, hid_acted, e_ready, e_biased, msg_ready, win_ready, added = (
            sem("hid_ready"), sem("hid_acted"), sem("e_ready"), sem("e_biased"), sem("msg_ready"),
            sem("win_ready"), sem("added"))
        far_src_landed, far_attr_landed = sem("far_src_landed"), sem("far_attr_landed")
        far_rows_landed = [sem(f"far_rows_landed{u}") for u in range(4)]
        far_hid_ready, far_hid_acted, far_e_ready, far_e_biased = (
            sem("far_hid_ready"), sem("far_hid_acted"), sem("far_e_ready"), sem("far_e_biased"))
        far_rel_ready, far_picked, far_win_ready, far_added = (
            sem("far_rel_ready"), sem("far_picked"), sem("far_win_ready"), sem("far_added"))
        cent_ready, square_ready, var_ready, std_ready, rstd_ready, norm_ready, low_ready, high_ready = (
            sem("cent_ready"), sem("square_ready"), sem("var_ready"), sem("std_ready"),
            sem("rstd_ready"), sem("norm_ready"), sem("low_ready"), sem("high_ready"))
        y_biased = sem("y_biased")
        y_ready, y_acted, h_ready, h_biased = sem("y_ready"), sem("y_acted"), sem("h_ready"), sem("h_biased")
        h_stored = sem("h_stored")
        affine_ready, final_ready = sem("affine_ready"), sem("final_ready")
        packed_moved = sem("packed_moved")

        passed = {e: sem(f"passed_{e}") for e in ("sp", "pool", "pe", "dve")}

        block = ctx.enter_context(nc.Block())
        ds = bass.ds

        assert 2 * NC + 2 * NG <= TPG * TN
        far_pick_flat = far_pick[:, :, :].rearrange("p t w -> p (t w)")

        def scratch(n):
            return far_pick_flat[:, n * NC:(n + 1) * NC]

        def own_wait(eng, name):
            eng.sem_inc(passed[name], 1)

        def low(t):
            return state[:, ds(t * 2 * TN, TN)]

        def high(t):
            return state[:, ds(t * 2 * TN + TN, TN)]

        def one(table, n):
            return table[ds(n, 1)].rearrange("a p c -> (a p) c")

        def rounds(eng, first, edges):
            first()
            with eng.Fori(0, L - 1) as l:
                edges(l, False)
            edges(L - 1, True)

        def rounds_by_parity(eng, first, edges):
            first()
            pairs = (L - 1) // 2
            if pairs:
                with eng.Fori(0, pairs) as p:
                    for parity in range(2):
                        edges(2 * p + parity, False, parity)
            for l in range(2 * pairs, L):
                edges(l, l == L - 1, l % 2)

        def node_tiles(eng, step):
            def peeled(t):
                step(t, t % 2, t + 2 < NT, 0 <= t + 1 < NT, 0 <= t < NT, t > 0)

            for t in range(-2, 2):
                peeled(t)
            if NPAIR > 2:
                with eng.Fori(1, NPAIR - 1) as i:
                    for j in range(2):
                        step(2 * i + j, j, True, True, True, True)
            for t in range(NT - 2, NT + 1):
                peeled(t)

        def edge_groups(eng, group):
            def iteration(i, afters):
                go = eng.value_load(tile_go[0:1, ds(i, 1)], min_val=0, max_val=1)
                t = eng.value_load(tile_at[0:1, ds(i, 1)], min_val=0, max_val=NT - 1)

                def step(body):
                    with eng.If(go > 0):
                        body(t)

                for u in range(RING):
                    group(i, u, afters[u], step)

            with eng.Fori(0, IT - 1) as i:
                iteration(i, [2] * RING)
            iteration(IT - 1, [min(2, RING - 1 - u) for u in range(RING)])

        def other_tiles(eng, body):
            begin = eng.value_load(tiles_in_loop[0:1, 0:1], min_val=0, max_val=NT - 1)
            with eng.Fori(begin, NT) as t:
                body(t)

        def if_far(eng, body):
            count = eng.value_load(far_count[0:1, 0:1], min_val=0, max_val=NG * GROUP)
            with eng.If(count > 0):
                body()

        @block.sync
        def _(sp):
            x_tiles = a["x_t"].rearrange("d (t s c) -> s d t c", s=2, c=TN)

            def load_x(begin, end, landed):
                for side in range(2):
                    to = x_packed[side * D:(side + 1) * D, begin * TN:end * TN]
                    sp.dma_start(to.rearrange("d (t c) -> d t c", c=TN),
                                 x_tiles[side][:, begin:end, :]).then_inc(landed, 16)

            load_x(0, 2, x_head_landed)
            sp.dma_start(node_w[:, :], one(a["node_pack"], 0)).then_inc(node_w_landed, 16)
            load_x(2, NT, packed_moved)
            sp.dma_start(edge_w[:, :], one(a["edge_pack"], 0)).then_inc(edge_w_landed, 16)
            sp.dma_start(start_i[:, :], a["starts"].to_broadcast((P, 2 * NG))).then_inc(start_landed, 16)
            sp.dma_start(scratch(0).bitcast(I32), a["dst_tiles"]).then_inc(dst_landed, 16)

            def load(g, u):
                sp.dma_start(src[:, u, :], one(a["src_tiles"], g)).then_inc(src_landed[u], 16)
                sp.dma_start(attr[:, u, :], one(a["attr_t"], g)).then_inc(attr_landed[u], 16)

            for u in range(RING):
                load(u, u)

            def store_h(k, t, parity):
                sp.wait_ge(h_biased, k * NT + t + 1)
                for side in range(2):
                    to = h_rows[parity][ds(t * 2 * TN + side * TN, TN), :]
                    sp.dma_start(to.rearrange("(p s) f -> p (s f)", s=SUB),
                                 h_out[:, side * SUB * D:(side + 1) * SUB * D]).then_inc(h_stored, 16)

            def store_y(t):
                sp.wait_ge(final_ready, t + 1)
                sp.dma_start(a["y"][:, ds(t * TN, TN)], final[:, :]).then_inc(packed_moved, 16)

            def first():
                store_h(0, 0, 0)
                with sp.Fori(1, NT) as t:
                    store_h(0, t, 0)
                sp.wait_ge(plan_ready, 2)

            def far_pass(l):
                with sp.Fori(0, NG) as g:
                    sp.wait_ge(far_added, (l * NG + g) * FW + 1)
                    sp.dma_start(far_src[:, :], one(a["src_tiles"], g)).then_inc(far_src_landed, 16)
                    sp.dma_start(far_attr[:, :], one(a["attr_t"], g)).then_inc(far_attr_landed, 16)
                sp.wait_ge(far_added, (l + 1) * NG * FW + 1)
                own_wait(sp, "sp")

            def edges(l, last, parity):
                sp.dma_start(ln_w[:, :], one(a["ln_pack"], l)).then_inc(ln_landed, 16)
                if not last:
                    sp.dma_start(node_w[:, :], one(a["node_pack"], l + 1)).then_inc(node_w_landed, 16)
                def store(t):
                    if last:
                        store_y(t)
                    else:
                        store_h(l + 1, t, 1 - parity)

                def group(i, u, after, step):
                    if after == 2 and not (isinstance(i, int) and i == IT - 1):
                        sp.wait_ge(msg_ready, l * NG + i * RING + u + 1)
                        load(i * RING + RING + u, u)
                    elif not last:
                        sp.wait_ge(msg_ready, l * NG + i * RING + u + 1)
                        load(u, u)
                    if u == RING - 1:
                        step(store)

                edge_groups(sp, group)
                if not last:
                    sp.wait_ge(added, 2 * NG * (l + 1) + 1)
                    own_wait(sp, "sp")
                if_far(sp, lambda: far_pass(l))
                if not last:
                    sp.dma_start(edge_w[:, :], one(a["edge_pack"], l + 1)).then_inc(edge_w_landed, 16)
                other_tiles(sp, store)

            rounds_by_parity(sp, first, edges)
            sp.wait_ge(packed_moved, 32 + 16 * NT)

        @block.gpsimd
        def _(pool):
            pool.iota(column_i[:, :], pattern=[[1, TN]], base=0, channel_multiplier=0).then_inc(column_ready, 1)
            pool.iota(part_i[:, :], pattern=[[0, 1]], base=0, channel_multiplier=1).then_inc(column_ready, 1)
            pool.wait_ge(filled, 11)
            pool.affine_select(out=center_both[:, :], in_=center_both[:, :], compare_op=ALU.not_equal,
                               fill=1.0 - 1.0 / D, base=0, pattern=[[-1, P]], channel_multiplier=1
                               ).then_inc(consts_ready, 1)
            for c in (0, 2):
                part = center[:, c * D:(c + 1) * D]
                pool.affine_select(out=part, in_=part, compare_op=ALU.not_equal, fill=1.0 - 1.0 / D,
                                   base=0, pattern=[[-1, D]], channel_multiplier=1).then_inc(consts_ready, 1)

            def gathers(table, index, to, landed, tiles=TPG):
                for j in range(TPH):
                    for side in range(2):
                        t, at = side * TPH + j, (2 * j + side) * D
                        if t >= tiles:
                            continue
                        pool.indirect_dma_start(
                            to[:, at:at + D], None, table,
                            bass.IndirectOffsetOnAxis(ap=index[:, t:t + 1], axis=0)).then_inc(landed(t), 16)

            def far_pass(l, table):
                with pool.Fori(0, NG) as g:
                    pool.wait_ge(far_src_landed, 16 * (l * NG + g + 1))
                    own_wait(pool, "pool")
                    gathers(table, far_src, far_rows, lambda t: far_rows_landed[t % 4])

            def edges(l, last, parity):
                table = h_rows[parity]
                pool.wait_ge(h_stored, 32 * NT * (l + 1))
                own_wait(pool, "pool")

                def group(i, u, tiles):
                    pool.wait_ge(src_landed[u], 16 * (l * IT + i + 1))
                    own_wait(pool, "pool")
                    gathers(table, src[:, u, :], rows[:, u, :], lambda t: rows_landed[u], tiles)

                with pool.Fori(0, IT - 1) as i:
                    for u in range(RING):
                        group(i, u, TPG)
                for u in range(RING):
                    group(IT - 1, u, last_tiles[u])
                pool.wait_ge(plan_ready, 2)
                own_wait(pool, "pool")
                if_far(pool, lambda: far_pass(l, table))

            rounds_by_parity(pool, lambda: None, edges)

        @block.tensor
        def _(pe):
            def centered(t, to):
                pe.matmul(to[:, 0:TN], center[:, 0:P], low(t), start=True, stop=False)
                pe.matmul(to[:, 0:TN], center[:, D:3 * D], high(t), start=False, stop=True
                          ).then_inc(cent_ready, 1)

            def variance(q, j, to):
                pe.wait_ge(square_ready, q + 1)
                pe.matmul(to[:, 0:TN], spread[:, :], square[:, j, :], start=True, stop=True
                          ).then_inc(var_ready, 1)

            def y(q, t, to):
                pe.wait_ge(low_ready, q + 1)
                own_wait(pe, "pe")
                pe.matmul(to[0][:, 0:TN], node_w[0:D, 0:H], low(t), start=True, stop=True).then_inc(y_ready, 1)
                pe.wait_ge(high_ready, q + 1)
                own_wait(pe, "pe")
                pe.matmul(to[1][:, 0:TN], node_w[0:D, 0:H], high(t), start=True, stop=True).then_inc(y_ready, 1)

            def h(q, to):
                for side in range(2):
                    pe.wait_ge(y_acted, 2 * q + side + 1)
                    for s in range(SUB):
                        at = (side * SUB + s) * D
                        mm = pe.matmul(to[0:ROWS, at:at + D], y_act[:, side, s:TN:SUB],
                                       node_w[:, H:H + D], start=True, stop=True)
                mm.then_inc(h_ready, 1)

            def first():
                pe.wait_ge(consts_ready, 3)
                pe.wait_ge(x_head_landed, 32)
                pe.wait_ge(node_w_landed, 16)

                def step(t, j, head, norm, mlp, rows):
                    if norm and not (isinstance(t, int) and t < 0):
                        pe.wait_ge(norm_ready, t + 1)
                        own_wait(pe, "pe")
                    if head:
                        if isinstance(t, int) and t == 0:
                            pe.wait_ge(packed_moved, 32)
                        pe.matmul(cent_ps[j][:, 0:TN], center_both[:, :], x_packed[:, ds((t + 2) * TN, TN)],
                                  start=True, stop=True).then_inc(cent_ready, 1)
                    if norm:
                        variance(t + 1, 1 - j, var_ps)
                    if rows:
                        h(t - 1, h_ps[1 - j])
                    if mlp:
                        y(t, t, y_ps)

                node_tiles(pe, step)
                pe.wait_ge(counted, 1)
                pe.matmul(win_ps[0][0:NT, 0:1], ones[:, :], far_sum[:, :], start=True, stop=True
                          ).then_inc(totalled, 1)
                pe.wait_ge(planned, 1)
                pe.matmul(win_ps[1][0:NT, 0:NT], ones[0:NT, :], plan[:, 2, 0:NT], start=True, stop=True
                          ).then_inc(plan_product, 1)
                pe.wait_ge(planned, 2)
                pe.matmul(tile_ps[0][0:1, 0:IT], due[:, 4:5], plan[:, 0, 0:IT], start=True, stop=True
                          ).then_inc(plan_product, 1)
                pe.wait_ge(plan_ready, 2)

            def edge_hidden(attributes, v):
                return pe.matmul(hid_ps[v][:, :], edge_w[0:2 * ED, 0:P], attributes, start=True, stop=True)

            def edge_out(v):
                for j in range(TPH):
                    mm = pe.matmul(e_ps[v][:, j * P:(j + 1) * P], hidden[:, v, j * TILE:(j + 1) * TILE],
                                   w2s[:, :], start=True, stop=True)
                return mm

            def far_pass(l):
                with pe.Fori(0, NG) as g:
                    n = l * NG + g
                    pe.wait_ge(far_attr_landed, 16 * (n + 1))
                    edge_hidden(far_attr[:, :], 0).then_inc(far_hid_ready, 1)
                    pe.wait_ge(far_hid_acted, n + 1)
                    edge_out(0).then_inc(far_e_ready, 1)
                    with pe.Fori(0, FW) as w:
                        pe.wait_ge(far_picked, n * FW + w + 1)
                        for t in range(TPG):
                            at = (2 * (t % TPH) + t // TPH) * D
                            mm = pe.matmul(far_ps[0:D, 0:TN], msg[:, at:at + D], far_pick[:, t, :],
                                           start=(t == 0), stop=(t == TPG - 1))
                        mm.then_inc(far_win_ready, 1)
                pe.wait_ge(far_added, (l + 1) * NG * FW + 1)
                own_wait(pe, "pe")

            def edges(l, last):
                pe.wait_ge(edge_w_landed, 16 * (l + 1))
                pe.wait_ge(w2s_ready, 2 * (l + 1))
                pe.wait_ge(h_biased, (l + 1) * NT)
                own_wait(pe, "pe")

                def hidden_of(u, use):
                    pe.wait_ge(attr_landed[u], 16 * (l * IT + use + 1))
                    edge_hidden(attr[:, u, :], u % 2).then_inc(hid_ready, 1)

                def out_of(n, v):
                    pe.wait_ge(hid_acted, n + 1)
                    edge_out(v).then_inc(e_ready, 1)

                hidden_of(0, 0)
                hidden_of(1, 0)
                out_of(l * NG, 0)

                def group(i, u, after, step):
                    n, v = l * NG + i * RING + u, u % 2
                    if u == 0:
                        step(lambda t: tile_centered(t, 2 * n + 1))
                    if u == 1:
                        step(tile_variance)
                    if after > 1:
                        hidden_of((u + 2) % RING, i + (u + 2) // RING)
                    if after > 0:
                        out_of(n + 1, 1 - v)
                    pe.wait_ge(msg_ready, n + 1)
                    for side in range(2):
                        for j in range(TPH):
                            at = (2 * j + side) * D
                            mm = pe.matmul(win_ps[side][0:D, 0:WIN], msg[:, at:at + D],
                                           pick[:, v, side * TPH + j, :], start=(j == 0), stop=(j == TPH - 1))
                        mm.then_inc(win_ready, 1)
                    if u == 2 and not last:
                        step(tile_y)
                    if u == 3 and not last:
                        step(tile_h)

                k = l + 1
                cent, var = tile_ps

                def tile_centered(t, sums):
                    pe.wait_ge(added, sums)
                    if last:
                        pe.wait_ge(norm_ready, k * NT + t)
                    else:
                        pe.wait_ge(h_biased, k * NT + t)
                    own_wait(pe, "pe")
                    centered(t, cent)

                def tile_variance(t):
                    variance(k * NT + t, 0, var)

                def tile_y(t):
                    pe.wait_ge(node_w_landed, 16 * (k + 1))
                    y(k * NT + t, t, [var, cent])

                def tile_h(t):
                    h(k * NT + t, var)

                edge_groups(pe, group)
                pe.wait_ge(added, 2 * NG * (l + 1) + 1)
                own_wait(pe, "pe")
                if_far(pe, lambda: far_pass(l))

                def tile(t):
                    tile_centered(t, 2 * NG * (l + 1) + 1)
                    tile_variance(t)
                    if not last:
                        tile_y(t)
                        tile_h(t)

                other_tiles(pe, tile)

            rounds(pe, first, edges)

        @block.scalar
        def _(act):
            act.wait_ge(eps_ready, 1)
            act.activation(warm[:, :], eps[:, :], ACT.Sqrt).then_inc(table_ready, 1)

            def squared(q, j, of):
                act.wait_ge(cent_ready, q + 1)
                act.activation(square[:, j, :], of[:, 0:TN], ACT.Square).then_inc(square_ready, 1)

            def root(q, of):
                act.wait_ge(var_ready, q + 1)
                act.activation(std[:, :], of[:, 0:TN], ACT.Sqrt, bias=eps[:, :]).then_inc(std_ready, 1)

            def biased(q, of):
                for side in range(2):
                    act.wait_ge(y_ready, 2 * q + side + 1)
                    act.activation(y_sum[:, side, :], of[side][:, 0:TN], ACT.Identity,
                                   bias=node_w[:, H + 2 * D:H + 2 * D + 1]).then_inc(y_biased, 1)

            def first():
                def positive(t):
                    act.wait_ge(norm_ready, t + 1)
                    act.activation(high(t), normed[D:P, :], ACT.Relu).then_inc(high_ready, 1)

                def step(t, j, head, norm, mlp, rows):
                    if norm:
                        root(t + 1, var_ps)
                    if head:
                        squared(t + 2, j, cent_ps[j])
                    if mlp:
                        biased(t, y_ps)
                    if norm:
                        positive(t + 1)

                node_tiles(act, step)
                act.wait_ge(plan_ready, 2)

            def hidden_biased(v):
                return act.activation(hid_sum[:, v, :], hid_ps[v][:, :], ACT.Identity,
                                      bias=edge_w[:, 2 * P + D:2 * P + D + 1])

            def far_pass(l):
                with act.Fori(0, NG) as g:
                    act.wait_ge(far_hid_ready, l * NG + g + 1)
                    hidden_biased(0).then_inc(far_hid_biased, 1)

            def edges(l, last):
                k = l + 1
                cent, var = tile_ps

                def edge_hidden(n, v):
                    act.wait_ge(hid_ready, n + 1)
                    hidden_biased(v).then_inc(hid_biased, 1)

                def tile_squared(t):
                    squared(k * NT + t, 0, cent)

                def tile_root(t):
                    root(k * NT + t, var)

                def tile_affine(t):
                    act.wait_ge(ln_landed, 16 * k)
                    if last:
                        act.wait_ge(packed_moved, 32 + 16 * t)
                    act.wait_ge(norm_ready, k * NT + t + 1)
                    if last:
                        act.activation(final[:, :], normed[:, :], ACT.Identity, scale=ln_w[:, 0:1],
                                       bias=ln_w[:, 1:2]).then_inc(affine_ready, 1)
                    else:
                        act.activation(high(t), normed[D:P, :], ACT.Identity, scale=ln_w[D:P, 0:1],
                                       bias=ln_w[D:P, 1:2]).then_inc(high_ready, 1)

                def tile_biased(t):
                    biased(k * NT + t, [var, cent])

                def group(i, u, after, step):
                    if u < 3:
                        step([tile_squared, tile_root, tile_affine][u])
                    elif not last:
                        step(tile_biased)
                    if after > 1:
                        edge_hidden(l * NG + i * RING + u + 2, u % 2)

                edge_hidden(l * NG, 0)
                edge_hidden(l * NG + 1, 1)
                edge_groups(act, group)
                if_far(act, lambda: far_pass(l))

                def tile(t):
                    tile_squared(t)
                    tile_root(t)
                    tile_affine(t)
                    if not last:
                        tile_biased(t)

                other_tiles(act, tile)

            rounds(act, first, edges)

        @block.vector
        def _(dve):
            dve.memset(eps[:, :], EPS).then_inc(eps_ready, 1)
            dve.memset(state[:, NPAD:NPAD + WIN], 0.0).then_inc(added, 1)
            dve.memset(ones[:, :], 1.0).then_inc(far_added, 1)
            dve.memset(center[:, D:2 * D], 0.0).then_inc(filled, 1)
            for c in (0, 2):
                dve.memset(center[:, c * D:(c + 1) * D], -1.0 / D).then_inc(filled, 1)
            for r in range(2):
                for c in range(2):
                    for matrix, mean in ((center_both, -1.0 / D), (spread, 1.0 / D)):
                        dve.memset(matrix[r * D:(r + 1) * D, c * D:(c + 1) * D], mean if r == c else 0.0
                                   ).then_inc(filled, 1)
            dve.wait_ge(column_ready, 2)
            dve.tensor_copy(column[:, :], column_i[:, :]).then_inc(column_ready, 1)
            dve.tensor_copy(part[:, :], part_i[:, :]).then_inc(column_ready, 1)

            start_f = far_pick_flat[:, 2 * NC:2 * NC + 2 * NG]

            def prepared(instruction, n):
                instruction.then_inc(prep, 1)
                dve.wait_ge(prep, n)

            def place_edges():
                inside, upper = scratch(0), scratch(1)

                dve.wait_ge(dst_landed, 16)
                prepared(dve.tensor_copy(far[:, :], scratch(0).bitcast(I32)), 1)
                dve.wait_ge(start_landed, 16)
                prepared(dve.tensor_copy(start_f, start_i[:, :]), 2)
                prepared(dve.tensor_tensor(rel[:, :].rearrange("p (h j) -> p h j", j=TPH),
                                           far[:, :].rearrange("p (h j) -> p h j", j=TPH),
                                           start_f.unsqueeze(2).to_broadcast((P, 2 * NG, TPH)), ALU.subtract), 3)
                prepared(dve.tensor_single_scalar(inside, rel[:, :], 0.0, ALU.is_ge), 4)
                prepared(dve.scalar_tensor_tensor(upper, rel[:, :], float(WIN), inside, ALU.is_lt, ALU.mult), 5)
                prepared(dve.scalar_tensor_tensor(inside, far[:, :], 1.0, upper, ALU.add, ALU.mult), 6)
                prepared(dve.tensor_tensor(far[:, :], far[:, :], inside, ALU.subtract), 7)
                prepared(dve.tensor_single_scalar(inside, far[:, :], 0.0, ALU.is_ge), 8)
                prepared(dve.scalar_tensor_tensor(upper, far[:, :], float(N), inside, ALU.is_lt, ALU.mult), 9)
                dve.reduce_sum(far_sum[:, :], upper, axis=mybir.AxisListType.X).then_inc(counted, 1)
                dve.wait_ge(totalled, 1)
                dve.tensor_copy(far_count[:, :], win_ps[0][0:1, 0:1]).then_inc(plan_ready, 1)

            def plan_tiles():
                ends, need, early, late, number = (due[:, c:c + 1] for c in range(5))
                iters = column[0:NT, 0:IT]
                prepared(dve.tensor_scalar(ends, part[0:NT, :], 2.0 * TN, 2.0 * TN + 1.0, ALU.mult, ALU.add), 10)
                prepared(dve.tensor_scalar(plan[:, 0, 0:2 * NG], start_f[0:NT, :], ends, None, ALU.is_lt), 11)
                prepared(dve.scalar_tensor_tensor(plan[:, 1, 0:2 * NG], column[0:NT, 0:2 * NG], 1.0,
                                                  plan[:, 0, 0:2 * NG], ALU.add, ALU.mult), 12)
                prepared(dve.reduce_max(need, plan[:, 1, 0:2 * NG], axis=mybir.AxisListType.X), 13)
                prepared(dve.tensor_scalar(plan[:, 0, 0:IT], iters, 1.0, 2.0 * RING, ALU.add, ALU.mult), 14)
                prepared(dve.tensor_scalar(plan[:, 1, 0:IT], plan[:, 0, 0:IT], need, None, ALU.is_lt), 15)
                prepared(dve.reduce_sum(early, plan[:, 1, 0:IT], axis=mybir.AxisListType.X), 16)
                prepared(dve.tensor_scalar(number, part[0:NT, :], 1.0, None, ALU.add), 17)
                dve.tensor_scalar(plan[:, 2, 0:NT], column[0:NT, 0:NT], part[0:NT, :], early,
                                  ALU.is_equal, ALU.mult).then_inc(planned, 1)
                prepared(dve.tensor_scalar(plan[:, 0, 0:NT], column[0:NT, 0:NT], part[0:NT, :], -1.0,
                                           ALU.subtract, ALU.mult), 18)
                prepared(dve.tensor_scalar(plan[:, 1, 0:NT], plan[:, 0, 0:NT], 0.0, -2.0 * TN,
                                           ALU.is_lt, ALU.mult), 19)
                prepared(dve.tensor_tensor(plan[:, 0, 0:NT], plan[:, 0, 0:NT], plan[:, 1, 0:NT], ALU.add), 20)
                dve.wait_ge(plan_product, 1)
                prepared(dve.tensor_tensor(plan[:, 1, 0:NT], plan[:, 0, 0:NT], win_ps[1][0:NT, 0:NT], ALU.add), 21)
                prepared(dve.reduce_max(late, plan[:, 1, 0:NT], axis=mybir.AxisListType.X), 22)
                prepared(dve.tensor_scalar(need, win_ps[0][0:NT, 0:1], 2.0 * TN, 1.0, ALU.mult, ALU.add), 23)
                prepared(dve.tensor_tensor(late, late, need, ALU.add), 24)
                dve.tensor_scalar(plan[:, 0, 0:IT], iters, late, None, ALU.is_equal).then_inc(planned, 1)
                dve.wait_ge(plan_product, 2)
                turn = tile_ps[0][0:1, 0:IT]
                dve.tensor_single_scalar(tile_go[:, :], turn, 0.0, ALU.is_gt)
                prepared(dve.tensor_scalar(tile_at[:, :], turn, -1.0, 0.0, ALU.add, ALU.max), 25)
                dve.reduce_max(tiles_in_loop[:, :], turn, axis=mybir.AxisListType.X).then_inc(plan_ready, 1)

            def leaky(out, y):
                return dve.scalar_tensor_tensor(out, y, SLOPE, y, ALU.mult, ALU.max)

            def normalize(q, of):
                dve.wait_ge(std_ready, q + 1)
                dve.reciprocal(rstd[:, :], std[:, :]).then_inc(rstd_ready, 1)
                dve.wait_ge(rstd_ready, q + 1)
                dve.tensor_tensor(normed[:, :], of[:, 0:TN], rstd[:, :], ALU.mult).then_inc(norm_ready, 1)

            def y_leaky(q):
                for side in range(2):
                    dve.wait_ge(y_biased, 2 * q + side + 1)
                    leaky(y_act[:, side, :], y_sum[:, side, :]).then_inc(y_acted, 1)

            def h_sum(q, of, stored):
                dve.wait_ge(h_ready, q + 1)
                if stored is not None:
                    dve.wait_ge(h_stored, stored)
                dve.tensor_tensor(h_out[:, :].rearrange("p (s f) -> p s f", f=D),
                                  of[0:ROWS, :].rearrange("p (s f) -> p s f", f=D),
                                  node_w[0:ROWS, H + D:H + 2 * D].unsqueeze(1).to_broadcast((ROWS, 2 * SUB, D)),
                                  ALU.add).then_inc(h_biased, 1)

            def first():
                def norm(t, j):
                    normalize(t, cent_ps[j])
                    dve.wait_ge(norm_ready, t + 1)
                    dve.tensor_single_scalar(low(t), normed[0:D, :], 0.0, ALU.max).then_inc(low_ready, 1)

                def step(t, j, head, norm_part, mlp, rows):
                    if norm_part:
                        norm(t + 1, 1 - j)
                    if rows:
                        h_sum(t - 1, h_ps[1 - j], None if isinstance(t, int) and t == 1 else 32 * (t - 1))
                    if mlp:
                        y_leaky(t)

                node_tiles(dve, step)
                place_edges()
                plan_tiles()
                dve.wait_ge(plan_ready, 2)

            def edge_biased(v):
                return dve.tensor_tensor(e_rows[:, v, :].rearrange("p (t f) -> p t f", f=D),
                                         e_ps[v][:, :].rearrange("p (t f) -> p t f", f=D),
                                         b2s[:, :].unsqueeze(1).to_broadcast((P, TPG, D)), ALU.add)

            def one_hot(out, width, where):
                return dve.tensor_tensor(out, column[:, 0:width].unsqueeze(1).to_broadcast((P, TPG, width)),
                                         where.unsqueeze(2).to_broadcast((P, TPG, width)), ALU.is_equal)

            def far_pass(l):
                with dve.Fori(0, NG) as g:
                    n = l * NG + g
                    dve.tensor_copy(far_rel[:, :], far[:, ds(g * TPG, TPG)]).then_inc(far_rel_ready, 1)
                    dve.wait_ge(far_hid_biased, n + 1)
                    leaky(hidden[:, 0, :], hid_sum[:, 0, :]).then_inc(far_hid_acted, 1)
                    dve.wait_ge(far_e_ready, n + 1)
                    edge_biased(0).then_inc(far_e_biased, 1)
                    dve.wait_ge(far_e_biased, n + 1)
                    for t in range(4):
                        dve.wait_ge(far_rows_landed[t], 32 * (n + 1))
                    dve.tensor_tensor(msg[:, :], far_rows[:, :], e_rows[:, 0, :], ALU.mult)
                    with dve.Fori(0, FW) as w:
                        m = n * FW + w
                        dve.wait_ge(far_rel_ready, n * (FW + 1) + w + 1)
                        one_hot(far_pick[:, :, :], TN, far_rel[:, :]).then_inc(far_picked, 1)
                        dve.wait_ge(far_picked, m + 1)
                        dve.tensor_scalar_add(far_rel[:, :], far_rel[:, :], -float(TN)).then_inc(far_rel_ready, 1)
                        dve.wait_ge(far_win_ready, m + 1)
                        dve.wait_ge(far_added, m + 1)
                        dve.tensor_tensor(state[:, ds(w * TN, TN)], state[:, ds(w * TN, TN)],
                                          far_ps[0:D, 0:TN], ALU.add).then_inc(far_added, 1)
                    dve.wait_ge(far_rel_ready, (n + 1) * (FW + 1))
                    own_wait(dve, "dve")

            def edges(l, last):
                dve.wait_ge(edge_w_landed, 16 * (l + 1))
                dve.tensor_tensor(scale[:, :], edge_w[:, 2 * P + D + 1:2 * P + D + 2],
                                  edge_w[:, 2 * P + D + 2:2 * P + D + 3], ALU.mult).then_inc(scale_ready, 1)
                dve.wait_ge(scale_ready, l + 1)
                dve.tensor_scalar_mul(w2s[:, :], edge_w[:, P:2 * P], scale[:, :]).then_inc(w2s_ready, 1)
                dve.tensor_scalar_mul(b2s[:, :], edge_w[:, 2 * P:2 * P + D], scale[:, :]).then_inc(w2s_ready, 1)
                dve.wait_ge(w2s_ready, 2 * (l + 1))
                own_wait(dve, "dve")
                def acted(n, v):
                    dve.wait_ge(hid_biased, n + 1)
                    leaky(hidden[:, v, :], hid_sum[:, v, :]).then_inc(hid_acted, 1)

                def out_biased(n, v):
                    dve.wait_ge(e_ready, n + 1)
                    edge_biased(v).then_inc(e_biased, 1)

                def picked(g, v):
                    one_hot(pick[:, v, :, :], WIN, rel[:, ds(g * TPG, TPG)])

                acted(l * NG, 0)
                acted(l * NG + 1, 1)
                out_biased(l * NG, 0)
                picked(0, 0)

                def group(i, u, after, step):
                    g, v = i * RING + u, u % 2
                    n = l * NG + g
                    starts = [dve.value_load(start_i[0:1, ds(2 * g + side, 1)], min_val=0, max_val=NPAD)
                              for side in range(2)]
                    dve.wait_ge(e_biased, n + 1)
                    if isinstance(i, int):
                        dve.wait_ge(rows_landed[u], rows_of_round[u] * (l + 1))
                    else:
                        dve.wait_ge(rows_landed[u], rows_of_round[u] * l + 16 * TPG * (i + 1))
                    dve.tensor_tensor(msg[:, :], rows[:, u, :], e_rows[:, v, :], ALU.mult).then_inc(msg_ready, 1)
                    if u == 3 and not last:
                        step(tile_leaky)
                    if after > 1:
                        acted(n + 2, v)
                    if after > 0:
                        out_biased(n + 1, 1 - v)
                        picked(g + 1, 1 - v)
                    for side in range(2):
                        dve.wait_ge(win_ready, 2 * n + side + 1)
                        dve.wait_ge(added, 2 * n + side + 1)
                        window = state[:, ds(starts[side], WIN)]
                        dve.tensor_tensor(window, window, win_ps[side][0:D, 0:WIN],
                                          ALU.add).then_inc(added, 1)
                    if u == 1:
                        step(tile_norm)
                    if u == 2 and last:
                        step(tile_final)
                    if u == 3 and not last:
                        step(tile_h)

                k = l + 1
                cent, var = tile_ps

                def tile_norm(t):
                    q = k * NT + t
                    normalize(q, cent)
                    if not last:
                        dve.wait_ge(ln_landed, 16 * k)
                        dve.wait_ge(norm_ready, q + 1)
                        dve.tensor_scalar(low(t), normed[0:D, :], ln_w[0:D, 0:1], ln_w[0:D, 1:2],
                                          ALU.mult, ALU.add).then_inc(low_ready, 1)

                def tile_final(t):
                    dve.wait_ge(affine_ready, t + 1)
                    dve.tensor_tensor(final[:, :], final[:, :], x_packed[:, ds(t * TN, TN)],
                                      ALU.add).then_inc(final_ready, 1)

                def tile_leaky(t):
                    y_leaky(k * NT + t)

                def tile_h(t):
                    h_sum(k * NT + t, var, 32 * (k * NT + t))

                edge_groups(dve, group)
                if_far(dve, lambda: far_pass(l))

                def tile(t):
                    tile_norm(t)
                    if last:
                        tile_final(t)
                    else:
                        tile_leaky(t)
                        tile_h(t)

                other_tiles(dve, tile)

            dve.wait_ge(column_ready, 4)
            rounds(dve, first, edges)

    return nc


def kernel(x, src, dst, edge_attr_32, L0_gnn_W1, L0_gnn_b1, L0_gnn_W2, L0_gnn_b2, L0_gnn_We1, L0_gnn_be1,
           L0_gnn_We2, L0_gnn_be2, L0_gnn_res_w, L0_gnn_dot_scale, L0_gnn_ln_g, L0_gnn_ln_b):
    import numpy as np
    import concourse.bacc as bacc
    from concourse.bass_utils import run_bass_kernel_spmd

    x, src, dst, attr, W1, b1, W2, b2, We1, be1, We2, be2, res, dot, g, b = (
        np.asarray(v) for v in (x, src, dst, edge_attr_32, L0_gnn_W1, L0_gnn_b1, L0_gnn_W2, L0_gnn_b2,
                                L0_gnn_We1, L0_gnn_be1, L0_gnn_We2, L0_gnn_be2, L0_gnn_res_w,
                                L0_gnn_dot_scale, L0_gnn_ln_g, L0_gnn_ln_b))
    (N, D), (E, ED), L = x.shape, attr.shape, W1.shape[0]
    NT, NPAD, NG = sizes(N, E)
    pad = NG * GROUP - E

    x_t = np.ascontiguousarray(np.pad(x, ((0, NPAD - N), (0, 0))).T)
    src_tiles = np.ascontiguousarray(np.pad(src, (0, pad)).reshape(NG, TPG, TILE).transpose(0, 2, 1))
    dst_all = np.pad(dst, (0, pad), constant_values=NPAD)
    dst_tiles = np.ascontiguousarray(dst_all.reshape(NG * TPG, TILE).T)
    starts = np.ascontiguousarray(dst_all.reshape(NG * 2, HALF)[:, 0][None, :])
    attr_t = np.ascontiguousarray(
        np.pad(attr, ((0, pad), (0, 0))).reshape(NG, 2, HALF, ED).transpose(0, 1, 3, 2).reshape(NG, 2 * ED, HALF))

    def on_rows(v):
        return np.broadcast_to(v[:, None, :], (L, P, v.shape[1]))

    def down(v):
        return np.concatenate([v, v], 1)[:, :, None]

    w1 = np.concatenate([W1, np.zeros_like(W1)], 1)
    node_pack = np.ascontiguousarray(np.concatenate([w1, W2, on_rows(b2), b1[:, :, None]], 2))
    we1 = np.zeros((L, P, P), x.dtype)
    we1[:, 0:ED, 0:D] = We1
    we1[:, ED:2 * ED, D:P] = We1
    we2 = np.zeros((L, P, P), x.dtype)
    we2[:, 0:D, 0:D] = We2
    we2[:, D:P, D:P] = We2
    edge_pack = np.ascontiguousarray(np.concatenate(
        [we1, we2, on_rows(be2), down(be1), on_rows(dot[:, None]), on_rows(res[:, None])], 2))
    ln_pack = np.ascontiguousarray(np.concatenate([down(g), down(b)], 2))

    arrays = dict(x_t=x_t, src_tiles=src_tiles, dst_tiles=dst_tiles, starts=starts, attr_t=attr_t,
                  node_pack=node_pack, edge_pack=edge_pack, ln_pack=ln_pack)
    nc = bacc.Bacc("TRN2", target_bir_lowering=False, num_devices=1)
    aps = {n: nc.dram_tensor(n, v.shape, mybir.dt.from_np(v.dtype), kind="ExternalInput").ap()
           for n, v in arrays.items()}
    aps["y"] = nc.dram_tensor("y", (P, NPAD // 2), F32, kind="ExternalOutput").ap()
    build(nc, aps, N, D, E, ED, L)
    y = run_bass_kernel_spmd(nc, [arrays], core_ids=[0]).results[0]["y"]
    return np.ascontiguousarray(y.reshape(2, D, NT, TN).transpose(2, 0, 3, 1).reshape(NPAD, D)[0:N])
```
